# Optimizing a Trainium2 kernel written in Bass

```python
import numpy as np
import jax
import jax.numpy as jnp

def _softmax(x, axis=-1):
    return jax.nn.softmax(x, axis=axis)

def _gelu(x):
    return jax.nn.gelu(x, approximate=True)

def _silu(x):
    return jax.nn.silu(x)

def _sigmoid(x):
    return jax.nn.sigmoid(x)

def _layernorm(x, axis=-1, eps=1e-05):
    m = jnp.mean(x, axis=axis, keepdims=True)
    v = jnp.var(x, axis=axis, keepdims=True)
    return (x - m) / jnp.sqrt(v + eps)

def _scatter_add(tgt, idx, src, axis=0):
    return tgt.at[idx].add(src)

def _segment_sum(src, seg, n):
    return jax.ops.segment_sum(src, seg, n)
kernel_name = 'mk_dlrm_tower_d1_rec_r8_b223d6'

def setup_inputs(seed: int=0):
    np.random.seed(seed)
    _w = jnp.asarray

    def _rec_inputs():
        import jax
        import jax.numpy as jnp
        _tk = jax.random.key(seed)
        ids = jnp.stack([jax.random.randint(jax.random.fold_in(_tk, 200 + f), (512,), 0, v, jnp.int32) for f, v in enumerate([1250, 1250, 1250, 12500, 1250, 12500, 12500, 125000, 1000, 12500, 1000, 12500, 12500, 1000, 1000, 1250, 1000, 1250, 12500, 12500, 1250, 1250, 1250, 1250, 1250, 1000])], axis=1)
        tbl_0 = 0.05 * jax.random.normal(jax.random.fold_in(_tk, 500 + 0), (1250, 128), jnp.float32)
        tbl_1 = 0.05 * jax.random.normal(jax.random.fold_in(_tk, 500 + 1), (1250, 128), jnp.float32)
        tbl_2 = 0.05 * jax.random.normal(jax.random.fold_in(_tk, 500 + 2), (1250, 128), jnp.float32)
        tbl_3 = 0.05 * jax.random.normal(jax.random.fold_in(_tk, 500 + 3), (12500, 128), jnp.float32)
        tbl_4 = 0.05 * jax.random.normal(jax.random.fold_in(_tk, 500 + 4), (1250, 128), jnp.float32)
        tbl_5 = 0.05 * jax.random.normal(jax.random.fold_in(_tk, 500 + 5), (12500, 128), jnp.float32)
        tbl_6 = 0.05 * jax.random.normal(jax.random.fold_in(_tk, 500 + 6), (12500, 128), jnp.float32)
        tbl_7 = 0.05 * jax.random.normal(jax.random.fold_in(_tk, 500 + 7), (125000, 128), jnp.float32)
        tbl_8 = 0.05 * jax.random.normal(jax.random.fold_in(_tk, 500 + 8), (1000, 128), jnp.float32)
        tbl_9 = 0.05 * jax.random.normal(jax.random.fold_in(_tk, 500 + 9), (12500, 128), jnp.float32)
        tbl_10 = 0.05 * jax.random.normal(jax.random.fold_in(_tk, 500 + 10), (1000, 128), jnp.float32)
        tbl_11 = 0.05 * jax.random.normal(jax.random.fold_in(_tk, 500 + 11), (12500, 128), jnp.float32)
        tbl_12 = 0.05 * jax.random.normal(jax.random.fold_in(_tk, 500 + 12), (12500, 128), jnp.float32)
        tbl_13 = 0.05 * jax.random.normal(jax.random.fold_in(_tk, 500 + 13), (1000, 128), jnp.float32)
        tbl_14 = 0.05 * jax.random.normal(jax.random.fold_in(_tk, 500 + 14), (1000, 128), jnp.float32)
        tbl_15 = 0.05 * jax.random.normal(jax.random.fold_in(_tk, 500 + 15), (1250, 128), jnp.float32)
        tbl_16 = 0.05 * jax.random.normal(jax.random.fold_in(_tk, 500 + 16), (1000, 128), jnp.float32)
        tbl_17 = 0.05 * jax.random.normal(jax.random.fold_in(_tk, 500 + 17), (1250, 128), jnp.float32)
        tbl_18 = 0.05 * jax.random.normal(jax.random.fold_in(_tk, 500 + 18), (12500, 128), jnp.float32)
        tbl_19 = 0.05 * jax.random.normal(jax.random.fold_in(_tk, 500 + 19), (12500, 128), jnp.float32)
        tbl_20 = 0.05 * jax.random.normal(jax.random.fold_in(_tk, 500 + 20), (1250, 128), jnp.float32)
        tbl_21 = 0.05 * jax.random.normal(jax.random.fold_in(_tk, 500 + 21), (1250, 128), jnp.float32)
        tbl_22 = 0.05 * jax.random.normal(jax.random.fold_in(_tk, 500 + 22), (1250, 128), jnp.float32)
        tbl_23 = 0.05 * jax.random.normal(jax.random.fold_in(_tk, 500 + 23), (1250, 128), jnp.float32)
        tbl_24 = 0.05 * jax.random.normal(jax.random.fold_in(_tk, 500 + 24), (1250, 128), jnp.float32)
        tbl_25 = 0.05 * jax.random.normal(jax.random.fold_in(_tk, 500 + 25), (1000, 128), jnp.float32)
        _rk = jax.random.fold_in(_tk, 7)
        r_dense = -0.000520686 + 1.00062 * jax.random.normal(jax.random.fold_in(_rk, 101), (512, 128), jnp.float32)
        W_top1 = 0.0456912 * jax.random.normal(jax.random.fold_in(_tk, 801), (479, 512), jnp.float32)
        W_top2 = 0.0441942 * jax.random.normal(jax.random.fold_in(_tk, 802), (512, 256), jnp.float32)
        W_top3 = 0.0625 * jax.random.normal(jax.random.fold_in(_tk, 803), (256, 1), jnp.float32)
        b_top1 = jnp.zeros((512,), jnp.float32)
        b_top2 = jnp.zeros((256,), jnp.float32)
        return (r_dense, ids, tbl_0, tbl_1, tbl_2, tbl_3, tbl_4, tbl_5, tbl_6, tbl_7, tbl_8, tbl_9, tbl_10, tbl_11, tbl_12, tbl_13, tbl_14, tbl_15, tbl_16, tbl_17, tbl_18, tbl_19, tbl_20, tbl_21, tbl_22, tbl_23, tbl_24, tbl_25, W_top1, b_top1, W_top2, b_top2, W_top3)
    r_dense, ids, tbl_0, tbl_1, tbl_2, tbl_3, tbl_4, tbl_5, tbl_6, tbl_7, tbl_8, tbl_9, tbl_10, tbl_11, tbl_12, tbl_13, tbl_14, tbl_15, tbl_16, tbl_17, tbl_18, tbl_19, tbl_20, tbl_21, tbl_22, tbl_23, tbl_24, tbl_25, W_top1, b_top1, W_top2, b_top2, W_top3 = _rec_inputs()

    def _L0_rec_setup():
        import jax, jax.numpy as jnp
        import numpy as np
        B, NUM_EMBS, D = (2048, 26, 128)
        key = jax.random.key(seed)
        k1, k2 = jax.random.split(key)
        dense = jax.random.normal(k1, (B, D), dtype=jnp.float32)
        embs = jax.random.normal(k2, (B, NUM_EMBS, D), dtype=jnp.float32)
        return {'dense': dense, 'embs': embs}
    _L0_rec_all = _L0_rec_setup()
    _L0_rec_in = {k: v for k, v in _L0_rec_all.items() if k in ()}
    del _L0_rec_all
    return {'r_dense': r_dense, 'ids': ids, 'tbl_0': tbl_0, 'tbl_1': tbl_1, 'tbl_2': tbl_2, 'tbl_3': tbl_3, 'tbl_4': tbl_4, 'tbl_5': tbl_5, 'tbl_6': tbl_6, 'tbl_7': tbl_7, 'tbl_8': tbl_8, 'tbl_9': tbl_9, 'tbl_10': tbl_10, 'tbl_11': tbl_11, 'tbl_12': tbl_12, 'tbl_13': tbl_13, 'tbl_14': tbl_14, 'tbl_15': tbl_15, 'tbl_16': tbl_16, 'tbl_17': tbl_17, 'tbl_18': tbl_18, 'tbl_19': tbl_19, 'tbl_20': tbl_20, 'tbl_21': tbl_21, 'tbl_22': tbl_22, 'tbl_23': tbl_23, 'tbl_24': tbl_24, 'tbl_25': tbl_25, 'W_top1': W_top1, 'b_top1': b_top1, 'W_top2': W_top2, 'b_top2': b_top2, 'W_top3': W_top3}

def reference(r_dense, ids, tbl_0, tbl_1, tbl_2, tbl_3, tbl_4, tbl_5, tbl_6, tbl_7, tbl_8, tbl_9, tbl_10, tbl_11, tbl_12, tbl_13, tbl_14, tbl_15, tbl_16, tbl_17, tbl_18, tbl_19, tbl_20, tbl_21, tbl_22, tbl_23, tbl_24, tbl_25, W_top1, b_top1, W_top2, b_top2, W_top3):
    import jax
    import jax.numpy as jnp

    def _L0_rec_ref(dense, embs):
        import jax, jax.numpy as jnp
        import numpy as np
        B, NUM_EMBS, D = (2048, 26, 128)
        T = jnp.concatenate([dense[:, None, :], embs], axis=1)
        N = T.shape[1]
        Z = jnp.einsum('bnd,bmd->bnm', T, T)
        iu0, iu1 = jnp.triu_indices(N, k=1)
        return Z[:, iu0, iu1]
    e = jnp.stack([tbl_0[ids[:, 0]], tbl_1[ids[:, 1]], tbl_2[ids[:, 2]], tbl_3[ids[:, 3]], tbl_4[ids[:, 4]], tbl_5[ids[:, 5]], tbl_6[ids[:, 6]], tbl_7[ids[:, 7]], tbl_8[ids[:, 8]], tbl_9[ids[:, 9]], tbl_10[ids[:, 10]], tbl_11[ids[:, 11]], tbl_12[ids[:, 12]], tbl_13[ids[:, 13]], tbl_14[ids[:, 14]], tbl_15[ids[:, 15]], tbl_16[ids[:, 16]], tbl_17[ids[:, 17]], tbl_18[ids[:, 18]], tbl_19[ids[:, 19]], tbl_20[ids[:, 20]], tbl_21[ids[:, 21]], tbl_22[ids[:, 22]], tbl_23[ids[:, 23]], tbl_24[ids[:, 24]], tbl_25[ids[:, 25]]], axis=1)
    z = _L0_rec_ref(r_dense, e)
    z = z.reshape(z.shape[0], -1)
    h = jnp.concatenate([z, r_dense], axis=1)
    h = jnp.maximum(h @ W_top1 + b_top1, 0.0)
    h = jnp.maximum(h @ W_top2 + b_top2, 0.0)
    y = h @ W_top3
    return y

_drawn_inputs = setup_inputs


def setup_inputs(seed=0):
    import zlib

    import numpy as np

    out = dict(_drawn_inputs(seed))
    spreads = {'b_top1': (0.0, 0.1), 'b_top2': (0.0, 0.1)}
    factors = {}
    for name, (base, spread) in spreads.items():
        noise = np.random.default_rng([zlib.crc32(name.encode()), seed]).standard_normal(out[name].shape)
        drawn = base * np.exp(spread * noise) if base else spread * noise
        out[name] = jnp.asarray(drawn.astype(out[name].dtype))
    for name, factor in factors.items():
        out[name] = (out[name] * factor).astype(out[name].dtype)
    return out
```

```python
from contextlib import ExitStack

import concourse.bass as bass
from concourse import mybir

F32 = mybir.dt.float32
I32 = mybir.dt.int32
U32 = mybir.dt.uint32
ALU = mybir.AluOpType
ACT = mybir.ActivationFunctionType

P = 128


def dlrm_tower(nc, dense, ids, tables, w1z, w1d, b1, w2, b2, w3, out):
    B, D = dense.shape
    NT = len(tables)
    NF = NT + 1
    T = B // P
    J, Q = 4, P // 4
    S, MM = 4, (NF + 3) // 4
    H1, H2 = w2.shape
    C1, C2 = H1 // P, H2 // P
    GF = 4
    groups = [list(range(g, min(g + GF, NF))) for g in range(0, NF, GF)]
    NG = len(groups)
    QB = Q // 2

    with ExitStack() as ctx:
        def sb(name, shape, dt=F32):
            return ctx.enter_context(nc.sbuf_tensor(name, shape, dt))

        def psum(name, shape):
            return ctx.enter_context(nc.psum_tensor(name, shape, F32))

        def sem(name):
            return ctx.enter_context(nc.semaphore(name))

        ids_sb = sb("ids_sb", [P, T, NT], I32)
        rows = sb("rows", [P, T, NF, D])
        feat = sb("feat", [P, B, NF])
        zt = sb("zt", [P, 2, MM, P])
        ident = sb("ident", [P, P])
        w1z_sb = sb("w1z_sb", [P, MM, H1])
        w1d_sb = sb("w1d_sb", [P, H1])
        b1_sb = sb("b1_sb", [P, C1])
        w2_sb = sb("w2_sb", [P, C1, H2])
        b2_sb = sb("b2_sb", [P, C2])
        w3_sb = sb("w3_sb", [P, C2])
        dT = sb("dT", [P, B])
        h1 = sb("h1", [P, C1, P])
        h2 = sb("h2", [P, C2, P])
        y_sb = sb("y_sb", [1, B])

        ps_t = psum("ps_t", [P, 2, 4 * P])
        ps_g = psum("ps_g", [P, 2, 512])
        ps_h1 = psum("ps_h1", [P, C1, P])
        ps_h2 = psum("ps_h2", [P, 512])

        ids_in = sem("ids_in")
        dense_in = sem("dense_in")
        w1_in = sem("w1_in")
        w2_in = sem("w2_in")
        gathered = [[sem(f"gathered_{t}_{g}") for g in range(NG)] for t in range(T)]
        ident_zeroed = sem("ident_zeroed")
        zt_zeroed = sem("zt_zeroed")
        ident_ready = sem("ident_ready")
        transposed = sem("transposed")
        evacuated = sem("evacuated")
        grams = sem("grams")
        z_taken = [sem(f"z_taken_{half}") for half in range(2)]
        l1_done = sem("l1_done")
        h1_ready = sem("h1_ready")
        l2_done = sem("l2_done")
        h2_ready = sem("h2_ready")
        l3_done = sem("l3_done")
        y_ready = sem("y_ready")
        out_done = sem("out_done")

        block = ctx.enter_context(nc.Block())

        @block.sync
        def _(sp):
            sp.dma_start(ids_sb[:], ids.rearrange("(t p) n -> p t n", p=P)).then_inc(ids_in, 16)
            sp.dma_start(rows[:, :, 0, :], dense.rearrange("(t p) d -> p t d", p=P)).then_inc(dense_in, 16)
            sp.dma_start(w1z_sb[:], w1z).then_inc(w1_in, 16)
            sp.dma_start(w1d_sb[:], w1d).then_inc(w1_in, 16)
            sp.dma_start(b1_sb[:], b1).then_inc(w1_in, 16)
            sp.dma_start(w2_sb[:], w2.rearrange("(c p) h -> p c h", p=P)).then_inc(w2_in, 16)
            sp.dma_start(b2_sb[:], b2).then_inc(w2_in, 16)
            sp.dma_start(w3_sb[:], w3).then_inc(w2_in, 16)
            sp.wait_ge(y_ready, T)
            sp.dma_start(out.rearrange("b o -> o b"), y_sb[:]).then_inc(out_done, 16)
            sp.wait_ge(out_done, 16)

        @block.gpsimd
        def _(pool):
            pool.wait_ge(ids_in, 16)
            for t in range(T):
                for g, fs in enumerate(groups):
                    for f in fs:
                        if f > 0:
                            pool.indirect_dma_start(
                                out=rows[:, t, f, :], out_offset=None, in_=tables[f - 1],
                                in_offset=bass.IndirectOffsetOnAxis(ap=ids_sb[:, t, f - 1:f].bitcast(U32), axis=0),
                            ).then_inc(gathered[t][g], 16)
                    if t == 0 and g == 0:
                        pool.memset(ident[:], 0.0).then_inc(ident_zeroed, 1)
                        pool.wait_ge(ident_zeroed, 1)
                        pool.affine_select(out=ident[:], in_=ident[:], compare_op=ALU.not_equal, fill=1.0, base=0,
                                           pattern=[[-1, P]], channel_multiplier=1).then_inc(ident_ready, 1)

        @block.tensor
        def _(pe):
            pe.wait_ge(ident_ready, 1)
            pe.wait_ge(dense_in, 16)

            def transposes(t):
                for g, fs in enumerate(groups):
                    n = t * NG + g
                    pe.wait_ge(gathered[t][g], 16 * len([f for f in fs if f > 0]))
                    if n >= 2:
                        pe.wait_ge(evacuated, n - 1)
                    for i, f in enumerate(fs):
                        last = pe.transpose(ps_t[:, n % 2, i * P:(i + 1) * P], rows[:, t, f, :], ident[:])
                    last.then_inc(transposed, 1)

            def gram(t):
                pe.wait_ge(evacuated, (t + 1) * NG)
                for half in range(2):
                    if t > 0:
                        pe.wait_ge(z_taken[half], t)
                    for q in range(QB):
                        for j in range(J):
                            b = t * P + 32 * j + half * QB + q
                            last = pe.matmul(ps_g[32 * j:32 * j + NF, half, q * NF:(q + 1) * NF],
                                             feat[:, b, :], feat[:, b, :], start=True, stop=True)
                    last.then_inc(grams, 1)

            def tower(t):
                if t == 0:
                    pe.wait_ge(w1_in, 48)
                else:
                    pe.wait_ge(h1_ready, t)
                for half in range(2):
                    pe.wait_ge(z_taken[half], t + 1)
                for c in range(C1):
                    for mm in range(MM):
                        pe.matmul(ps_h1[:, c, :], w1z_sb[:, mm, c * P:(c + 1) * P], zt[:, t % 2, mm, :],
                                  start=(mm == 0), stop=False)
                    last = pe.matmul(ps_h1[:, c, :], w1d_sb[:, c * P:(c + 1) * P], feat[:, t * P:(t + 1) * P, 0],
                                     start=False, stop=True)
                last.then_inc(l1_done, 1)
                if t == 0:
                    pe.wait_ge(w2_in, 48)
                pe.wait_ge(h1_ready, t + 1)
                if t > 0:
                    pe.wait_ge(y_ready, t)
                for c2 in range(C2):
                    for c in range(C1):
                        last = pe.matmul(ps_h2[:, c2 * P:(c2 + 1) * P], w2_sb[:, c, c2 * P:(c2 + 1) * P], h1[:, c, :],
                                         start=(c == 0), stop=(c == C1 - 1))
                last.then_inc(l2_done, 1)
                pe.wait_ge(h2_ready, t + 1)
                for c2 in range(C2):
                    last = pe.matmul(ps_h2[0:1, C2 * P:(C2 + 1) * P], w3_sb[:, c2:c2 + 1], h2[:, c2, :],
                                     start=(c2 == 0), stop=(c2 == C2 - 1))
                last.then_inc(l3_done, 1)

            for t in range(T):
                transposes(t)
                gram(t)
                tower(t)

        def z_copy(copy, t, half):
            for s in range(S):
                k = len(range(s, NF, 4))
                for j in range(J):
                    src = ps_g[32 * j:32 * j + NF, half, 0:QB * NF].rearrange("p (q m) -> p m q", m=NF)[:, s:NF:4, :]
                    b0 = 32 * j + half * QB
                    dst = zt[32 * s:32 * s + NF, t % 2, 0:k, b0:b0 + QB]
                    last = copy(dst, src)
            last.then_inc(z_taken[half], 1)

        @block.vector
        def _(dve):
            dve.memset(zt[:], 0.0).then_inc(zt_zeroed, 1)
            dve.wait_ge(zt_zeroed, 1)
            for t in range(T):
                for g, fs in enumerate(groups):
                    n = t * NG + g
                    dve.wait_ge(transposed, n + 1)
                    dve.tensor_copy(feat[:, t * P:(t + 1) * P, fs[0]:fs[-1] + 1].rearrange("p b f -> p f b"),
                                    ps_t[:, n % 2, 0:len(fs) * P].rearrange("p (f b) -> p f b", b=P),
                                    ).then_inc(evacuated, 1)
                if t >= 2:
                    dve.wait_ge(l1_done, t - 1)
                dve.wait_ge(grams, 2 * t + 1)
                z_copy(dve.tensor_copy, t, 0)

        @block.scalar
        def _(act):
            act.wait_ge(zt_zeroed, 1)
            for t in range(T):
                if t >= 2:
                    act.wait_ge(l1_done, t - 1)
                act.wait_ge(grams, 2 * t + 2)
                z_copy(act.copy, t, 1)
                act.wait_ge(l1_done, t + 1)
                if t > 0:
                    act.wait_ge(l2_done, t)
                else:
                    act.wait_ge(w1_in, 48)
                for c in range(C1):
                    last = act.activation(h1[:, c, :], ps_h1[:, c, :], ACT.Relu, bias=b1_sb[:, c:c + 1])
                last.then_inc(h1_ready, 1)
                act.wait_ge(l2_done, t + 1)
                if t > 0:
                    act.wait_ge(l3_done, t)
                else:
                    act.wait_ge(w2_in, 48)
                for c2 in range(C2):
                    last = act.activation(h2[:, c2, :], ps_h2[:, c2 * P:(c2 + 1) * P], ACT.Relu, bias=b2_sb[:, c2:c2 + 1])
                last.then_inc(h2_ready, 1)
                act.wait_ge(l3_done, t + 1)
                act.copy(y_sb[:, t * P:(t + 1) * P], ps_h2[0:1, C2 * P:(C2 + 1) * P]).then_inc(y_ready, 1)


def kernel(**inputs):
    import numpy as np
    import concourse.bacc as bacc
    from concourse import mybir as mb
    from concourse.bass_utils import run_bass_kernel_spmd

    names = [f"tbl_{i}" for i in range(sum(n.startswith("tbl_") for n in inputs))]
    nf = len(names) + 1
    w1 = np.asarray(inputs["W_top1"])
    h1 = w1.shape[1]
    n0, m0 = np.triu_indices(nf, k=1)
    w1z = np.zeros((128, (nf + 3) // 4, h1), w1.dtype)
    w1z[32 * (m0 % 4) + n0, m0 // 4] = w1[:len(n0)]
    arrays = {
        "dense": inputs["r_dense"], "ids": inputs["ids"],
        **{n: inputs[n] for n in names},
        "w1z": w1z, "w1d": w1[len(n0):], "b1": np.asarray(inputs["b_top1"]).reshape(-1, 128).T,
        "w2": inputs["W_top2"], "b2": np.asarray(inputs["b_top2"]).reshape(-1, 128).T,
        "w3": np.asarray(inputs["W_top3"]).reshape(-1, 128).T,
    }
    arrays = {n: np.ascontiguousarray(a) for n, a in arrays.items()}
    nc = bacc.Bacc("TRN2", target_bir_lowering=False, num_devices=1)
    a = {n: nc.dram_tensor(n, x.shape, mb.dt.from_np(x.dtype), kind="ExternalInput").ap() for n, x in arrays.items()}
    out = nc.dram_tensor("out", (arrays["dense"].shape[0], 1), mb.dt.float32, kind="ExternalOutput").ap()
    dlrm_tower(nc, a["dense"], a["ids"], [a[n] for n in names], a["w1z"], a["w1d"], a["b1"], a["w2"], a["b2"], a["w3"], out)
    r = run_bass_kernel_spmd(nc, [arrays], core_ids=[0])
    return r.results[0]["out"]
```

```python
from contextlib import ExitStack

import concourse.bass as bass
from concourse import mybir

F32 = mybir.dt.float32
F32R = mybir.dt.float32r
I32 = mybir.dt.int32
U32 = mybir.dt.uint32
ALU = mybir.AluOpType
ACT = mybir.ActivationFunctionType

P = 128
QUAD = 4
GROUP = 4
EARLY = (3, 5, 6)
WARMING = 16
TABLES = 3
RING = 16
ACT_CHUNKS = 1


def table_split(rows):
    n = next(n for n in range(P, 0, -1) if rows % n == 0)
    return n, rows // n


def dlrm_tower(nc, dense, ids, ids_by_table, gathered_tables, picked_tables, table_of_slot,
               w1z, w1d, w2, b2, w3, out):
    B, D = dense.shape
    NG, NK = len(gathered_tables), len(picked_tables)
    NF = 1 + NG + NK
    NM = NF - 1
    T = B // P
    TQ = P // QUAD
    QROW = QUAD * NM
    BANK_QUADS = 512 // QROW
    GJOBS = TQ // BANK_QUADS
    MM = (NM + 3) // 4
    H1, H2 = w2.shape
    C1 = H1 // P
    slots = [list(range(g, min(g + GROUP, 1 + NG))) for g in range(0, 1 + NG, GROUP)]
    TG = len(slots)
    splits = [table_split(tb.shape[0]) for tb in picked_tables]
    KP, CMAX = max(n for n, _ in splits), max(c for _, c in splits)
    W = 32

    with ExitStack() as ctx:
        def sb(name, shape, dt=F32):
            return ctx.enter_context(nc.sbuf_tensor(name, shape, dt))

        def psum(name, shape):
            return ctx.enter_context(nc.psum_tensor(name, shape, F32))

        def sem(name):
            return ctx.enter_context(nc.semaphore(name))

        ids_sb = sb("ids_sb", [P, T, ids.shape[1]], I32)
        rows = sb("rows", [P, 2, 1 + NG, D])
        feat = sb("feat", [P, T, P, W])
        ident = sb("ident", [P, P])
        warm = sb("warm", [P, P])
        w1z_sb = sb("w1z_sb", [P, MM, H1])
        w1z_hi = sb("w1z_hi", [P, MM, H1], F32R)
        w1d_sb = sb("w1d_sb", [P, H1])
        w2_sb = sb("w2_sb", [P, C1, H2])
        b2_sb = sb("b2_sb", [P, H2])
        w3_sb = sb("w3_sb", [P, H2])
        h1 = sb("h1", [P, H1])
        h1t = sb("h1t", [P, C1, P])
        h2 = sb("h2", [P, H2])
        h2w = sb("h2w", [P, H2])
        y = sb("y", [P, T])
        row_ids_int = sb("row_ids_int", [P, CMAX], I32)
        row_ids = {c: sb(f"row_ids_{c}", [P, c]) for c in sorted({c for _, c in splits})}

        with ExitStack() as of_picks:
            def pick_sb(name, shape, dt=F32):
                return of_picks.enter_context(nc.sbuf_tensor(name, shape, dt))

            ids_bc = pick_sb("ids_bc", [P, 2, B], I32)
            distance = pick_sb("distance", [P, B])
            table = pick_sb("table", [P, 2, CMAX * D])
            table_hi = pick_sb("table_hi", [P, TABLES, CMAX * D], F32R)
            table_lo = pick_sb("table_lo", [P, TABLES, CMAX * D], F32R)
            onehot = pick_sb("onehot", [P, RING, B], F32R)
        w1z_lo = sb("w1z_lo", [P, MM, H1], F32R)
        gram_hi = sb("gram_hi", [P, TQ, QROW], F32R)
        gram_lo = sb("gram_lo", [P, TQ, QROW], F32R)
        z_hi = sb("z_hi", [P, MM, P], F32R)
        z_lo = sb("z_lo", [P, MM, P], F32R)

        ps_t = psum("ps_t", [P, 2, GROUP * P])
        ps_g = psum("ps_g", [P, 3, 512])
        ps_h1 = psum("ps_h1", [P, H1])
        ps_h1t = psum("ps_h1t", [P, C1, P])
        ps_h2 = psum("ps_h2", [P, 512])

        ids_in = sem("ids_in")
        ids_bc_in = [sem(f"ids_bc_in_{n}") for n in range(2)]
        dense_in = [sem(f"dense_in_{n}") for n in range(2)]
        table_in = [sem(f"table_in_{n}") for n in range(2)]
        w1z_in = [sem(f"w1z_in_{n}") for n in range(2)]
        w1d_in = sem("w1d_in")
        w2_in = sem("w2_in")
        gathered = [[sem(f"gathered_{t}_{g}") for g in range(TG)] for t in range(T)]
        ident_zeroed = sem("ident_zeroed")
        ident_ready = sem("ident_ready")
        pads_zeroed = sem("pads_zeroed")
        z_filled = sem("z_filled")
        w1_hi_ready = sem("w1_hi_ready")
        w1_lo_ready = sem("w1_lo_ready")
        ids_made = sem("ids_made")
        row_ids_ready = sem("row_ids_ready")
        warm_ready = sem("warm_ready")
        hi_ready = sem("hi_ready")
        lo_ready = sem("lo_ready")
        onehot_ready = [sem(f"onehot_ready_{n}") for n in range(2)]
        distance_ready = sem("distance_ready")
        onehot_used = sem("onehot_used")
        picked_taken = sem("picked_taken")
        transposed = sem("transposed")
        turned = [sem(f"turned_{n}") for n in range(2)]
        products = sem("products")
        products_hi = sem("products_hi")
        products_taken = sem("products_taken")
        z_hi_ready = [sem(f"z_hi_ready_{n}") for n in range(2)]
        z_lo_ready = [sem(f"z_lo_ready_{n}") for n in range(2)]
        l1_done = sem("l1_done")
        h1_ready = sem("h1_ready")
        h1_transposed = sem("h1_transposed")
        h1t_ready = sem("h1t_ready")
        l2_done = sem("l2_done")
        h2_sum = sem("h2_sum")
        h2_ready = sem("h2_ready")
        y_ready = sem("y_ready")
        out_done = sem("out_done")

        def chunk(k, i):
            return sum(c for _, c in splits[:k]) + i

        def wait_picked(eng, k):
            eng.wait_ge(onehot_used, chunk(k, splits[k][1]))

        def wait_chunk_free(eng, k, i):
            if chunk(k, i) >= RING:
                eng.wait_ge(onehot_used, chunk(k, i) - RING + 1)

        def chunks_until(k, i, who):
            act_from = splits[k][1] - ACT_CHUNKS
            before = sum(c - ACT_CHUNKS if who == 0 else ACT_CHUNKS for _, c in splits[:k])
            return before + (min(i + 1, act_from) if who == 0 else max(0, i + 1 - act_from))

        halves = (slice(0, MM // 2), slice(MM // 2, MM))

        block = ctx.enter_context(nc.Block())

        def steps(pick, turn, product, l1, turn_h1, l2, copies_turns=True):
            for k in range(NK):
                pick(k)
                if 0 < k <= TG:
                    turn(0, k - 1)
            for g in range(NK - 1, TG):
                turn(0, g)
            for t in range(T):
                for n in range(GJOBS):
                    product(t, n)
                    if n == 0 and t > 0:
                        turn_h1(t - 1)
                    if n in EARLY and t + 1 < T:
                        turn(t + 1, EARLY.index(n))
                if t > 0:
                    l2(t - 1)
                if t + 1 < T:
                    for g in range(len(EARLY), TG - 1):
                        turn(t + 1, g)
                l1(t)
                if t + 1 < T and copies_turns:
                    turn(t + 1, TG - 1)
            turn_h1(T - 1)
            l2(T - 1)

        def nothing(*_):
            pass

        @block.sync
        def _(sp):
            def load_table(k):
                n, c = splits[k]
                if k >= 2:
                    for who in range(2):
                        sp.wait_ge(onehot_ready[who], chunks_until(k - 2, splits[k - 2][1] - 1, who))
                    sp.wait_ge(hi_ready, k - 1)
                    sp.wait_ge(lo_ready, k - 1)
                src = picked_tables[k].rearrange("(p c) d -> p (c d)", c=c)
                cut = n // 16 * 16
                sp.dma_start(table[0:cut, k % 2, 0:c * D], src[0:cut, :]).then_inc(table_in[k % 2], 16)
                if cut < n:
                    sp.dma_start(table[cut:n, k % 2, 0:c * D], src[cut:n, :]).then_inc(table_in[k % 2], 16)
                sp.dma_start(ids_bc[:, k % 2, :], ids_by_table[k:k + 1, :].to_broadcast([P, B])).then_inc(ids_bc_in[k % 2], 16)

            load_table(0)
            load_table(1)
            for t in range(2):
                sp.dma_start(rows[:, t, 0, :], dense[t * P:(t + 1) * P, :]).then_inc(dense_in[t], 16)
            for k in range(2, NK):
                load_table(k)
            for n, half in enumerate(halves):
                sp.dma_start(w1z_sb[:, half, :], w1z[:, half, :]).then_inc(w1z_in[n], 16)
            sp.dma_start(w1d_sb[:], w1d).then_inc(w1d_in, 16)
            sp.dma_start(w2_sb[:], w2.rearrange("(c p) h -> p c h", p=P)).then_inc(w2_in, 16)
            sp.dma_start(b2_sb[:], b2.to_broadcast([P, H2])).then_inc(w2_in, 16)
            sp.dma_start(w3_sb[:], w3.to_broadcast([P, H2])).then_inc(w2_in, 16)
            for t in range(2, T):
                sp.wait_ge(transposed, TG * (t - 2) + 1)
                sp.dma_start(rows[:, t % 2, 0, :], dense[t * P:(t + 1) * P, :]).then_inc(dense_in[t % 2], 16)
            for t in range(T):
                sp.wait_ge(y_ready, t + 1)
                sp.dma_start(out[t * P:(t + 1) * P, :], y[:, t:t + 1]).then_inc(out_done, 16)
            sp.wait_ge(out_done, 16 * T)

        @block.gpsimd
        def _(pool):
            for n, (c, tile) in enumerate(row_ids.items()):
                if n > 0:
                    pool.wait_ge(row_ids_ready, n)
                pool.iota(row_ids_int[:, 0:c], pattern=[[1, c]], base=0, channel_multiplier=c).then_inc(ids_made, 1)
                pool.wait_ge(ids_made, n + 1)
                pool.tensor_copy(tile[:], row_ids_int[:, 0:c]).then_inc(row_ids_ready, 1)
            pool.wait_ge(ids_in, 16)
            for t in range(T):
                for g, ss in enumerate(slots):
                    if t >= 2:
                        pool.wait_ge(transposed, TG * (t - 2) + g + 1)
                    for s in ss:
                        if s > 0:
                            i = table_of_slot[s]
                            pool.indirect_dma_start(
                                out=rows[:, t % 2, s, :], out_offset=None, in_=gathered_tables[s - 1],
                                in_offset=bass.IndirectOffsetOnAxis(ap=ids_sb[:, t, i:i + 1].bitcast(U32), axis=0),
                            ).then_inc(gathered[t][g], 16)
                    if t == 0 and g == 0:
                        pool.memset(ident[:], 0.0).then_inc(ident_zeroed, 1)
                        pool.wait_ge(ident_zeroed, 1)
                        pool.affine_select(out=ident[:], in_=ident[:], compare_op=ALU.not_equal, fill=1.0, base=0,
                                           pattern=[[-1, P]], channel_multiplier=1).then_inc(ident_ready, 1)

        def bank(job):
            return job % 3

        def wait_bank(eng, job):
            last = job - 3
            if last < 0:
                return
            if last < NK:
                eng.wait_ge(picked_taken, last + 1)
            else:
                eng.wait_ge(products_taken, last - NK + 1)

        def turner(n):
            return 1 if n < TG else (TG - 1 - n % TG) % 2

        def wait_turned(eng, n):
            eng.wait_ge(turned[turner(n)], len([i for i in range(n + 1) if turner(i) == turner(n)]))

        def turned_out(eng, copy, t, g, who):
            n, ss = t * TG + g, slots[g]
            if turner(n) == who:
                eng.wait_ge(transposed, n + 1)
                copy(feat[:, t, :, ss[0]:ss[-1] + 1].rearrange("p b f -> p f b"),
                     ps_t[:, n % 2, 0:len(ss) * P].rearrange("p (f b) -> p f b", b=P)).then_inc(turned[who], 1)

        @block.tensor
        def _(pe):
            pe.wait_ge(warm_ready, 1)
            for _ in range(WARMING):
                pe.matmul(ps_h1[:, 0:P], warm[:], warm[:], start=True, stop=True)

            def pick(k):
                n, c = splits[k]
                pe.wait_ge(hi_ready, k + 1)
                wait_bank(pe, k)
                order = ([(i, 0) for i in range(c)] + [(i, 1) for i in range(c)] if k == 0 else
                         [(i, part) for i in range(c) for part in range(2)])
                for m, (i, part) in enumerate(order):
                    if part == 0:
                        who = int(i >= c - ACT_CHUNKS)
                        pe.wait_ge(onehot_ready[who], chunks_until(k, i, who))
                    elif i == 0:
                        pe.wait_ge(lo_ready, k + 1)
                    mm = pe.matmul(ps_g[:, bank(k), :], (table_hi, table_lo)[part][0:n, k % TABLES, i * D:(i + 1) * D],
                                   onehot[0:n, chunk(k, i) % RING, :], start=(m == 0), stop=(m == 2 * c - 1))
                    if part == 1:
                        mm.then_inc(onehot_used, 1)

            def turn(t, g):
                n, ss = t * TG + g, slots[g]
                if n == 0:
                    pe.wait_ge(ident_ready, 1)
                if g == 0:
                    pe.wait_ge(dense_in[t % 2], 16 * (t // 2 + 1))
                pe.wait_ge(gathered[t][g], 16 * len([s for s in ss if s > 0]))
                if n >= 2:
                    wait_turned(pe, n - 2)
                for i, s in enumerate(ss):
                    last = pe.transpose(ps_t[:, n % 2, i * P:(i + 1) * P], rows[:, t % 2, s, :], ident[:])
                last.then_inc(transposed, 1)

            def product(t, n):
                if n == 0:
                    if t == 0:
                        pe.wait_ge(picked_taken, NK)
                        pe.wait_ge(pads_zeroed, 1)
                    wait_turned(pe, (t + 1) * TG - 1)
                    wait_turned(pe, (t + 1) * TG - 2)
                job = NK + t * GJOBS + n
                wait_bank(pe, job)
                for q in range(BANK_QUADS):
                    b = QUAD * (n * BANK_QUADS + q)
                    quad_all = feat[:, t, b:b + QUAD, :].rearrange("p b f -> p (b f)")
                    quad_used = feat[:, t, b:b + QUAD, 1:NF]
                    last = pe.matmul(ps_g[:, bank(job), q * QROW:(q + 1) * QROW], quad_all, quad_used,
                                     start=True, stop=True)
                last.then_inc(products, 1)

            def l1(t):
                if t == 0:
                    pe.wait_ge(w1d_in, 16)
                else:
                    pe.wait_ge(h1_ready, t)
                pe.matmul(ps_h1[:], feat[:, t, :, 0], w1d_sb[:], start=True, stop=False)
                if t == 0:
                    pe.wait_ge(w1_lo_ready, 2)
                for ready, z, weights in ((z_hi_ready, z_hi, (w1z_hi, w1z_lo)), (z_lo_ready, z_lo, (w1z_hi,))):
                    for n in range(2):
                        pe.wait_ge(ready[n], t + 1)
                    for mm in range(MM):
                        if z is z_lo and mm == MM // 2 and t + 1 < T:
                            turn(t + 1, TG - 1)
                        for w in weights:
                            last = pe.matmul(ps_h1[:], z[:, mm, :], w[:, mm, :], start=False,
                                             stop=(z is z_lo and mm == MM - 1))
                last.then_inc(l1_done, 1)

            def turn_h1(t):
                pe.wait_ge(h1_ready, t + 1)
                if t > 0:
                    pe.wait_ge(h1t_ready, t)
                for c in range(C1):
                    last = pe.transpose(ps_h1t[:, c, :], h1[:, c * P:(c + 1) * P], ident[:])
                last.then_inc(h1_transposed, 1)

            def l2(t):
                if t == 0:
                    pe.wait_ge(w2_in, 48)
                else:
                    pe.wait_ge(h2_sum, t)
                pe.wait_ge(h1t_ready, t + 1)
                for c in range(C1):
                    last = pe.matmul(ps_h2[:, 0:H2], h1t[:, c, :], w2_sb[:, c, :], start=(c == 0), stop=(c == C1 - 1))
                last.then_inc(l2_done, 1)

            steps(pick, turn, product, l1, turn_h1, l2, copies_turns=False)

        def bank_products(job):
            return ps_g[:, bank(NK + job), 0:BANK_QUADS * QROW].rearrange("p (q c) -> p q c", c=QROW)

        def pairs_out(eng, copy, t, who):
            if t > 0:
                eng.wait_ge(l1_done, t)
            for gram, z, ready, there in ((gram_hi, z_hi, z_hi_ready, products_hi),
                                          (gram_lo, z_lo, z_lo_ready, products_taken)):
                eng.wait_ge(there, (t + 1) * GJOBS)
                for s in range(4):
                    k = len(range(s, NM, 4))
                    for i in range(QUAD):
                        if (i + s) % 2 == who:
                            src = gram[32 * i:32 * i + NF, :, i * NM:(i + 1) * NM][:, :, s:NM:4]
                            dst = z[32 * s:32 * s + NF, 0:k, :].rearrange("p m (q i) -> p m q i", i=QUAD)[:, :, :, i]
                            last = copy(dst, src.rearrange("p q m -> p m q"))
                last.then_inc(ready[who], 1)

        @block.vector
        def _(dve):
            def pick(k):
                n, c = splits[k]
                if k == 0:
                    dve.memset(warm[:], 0.0).then_inc(warm_ready, 1)
                    dve.memset(feat[:, :, :, NF:W], 0.0).then_inc(pads_zeroed, 1)
                    dve.wait_ge(row_ids_ready, len(row_ids))
                dve.wait_ge(ids_bc_in[k % 2], 16 * (k // 2 + 1))
                for i in range(c - ACT_CHUNKS):
                    wait_chunk_free(dve, k, i)
                    dve.tensor_scalar(onehot[0:n, chunk(k, i) % RING, :], ids_bc[0:n, k % 2, :],
                                      row_ids[c][0:n, i:i + 1], None, ALU.is_equal).then_inc(onehot_ready[0], 1)
                    if i == (4 if k == 0 else 1):
                        dve.wait_ge(hi_ready, k + 1)
                        if k >= TABLES:
                            wait_picked(dve, k - TABLES)
                        dve.tensor_tensor(table_lo[0:n, k % TABLES, 0:c * D], table[0:n, k % 2, 0:c * D],
                                          table_hi[0:n, k % TABLES, 0:c * D].bitcast(F32), ALU.subtract).then_inc(lo_ready, 1)

            def turn(t, g):
                turned_out(dve, dve.tensor_copy, t, g, 0)

            def product(t, n):
                if t == 0 and n == 0:
                    for who in range(2):
                        dve.wait_ge(onehot_ready[who], chunks_until(NK - 1, splits[-1][1] - 1, who))
                    dve.wait_ge(lo_ready, NK)
                    for i, half in enumerate(halves):
                        dve.wait_ge(w1_hi_ready, i + 1)
                        dve.tensor_tensor(w1z_lo[:, half, :], w1z_sb[:, half, :], w1z_hi[:, half, :].bitcast(F32),
                                          ALU.subtract).then_inc(w1_lo_ready, 1)
                job = t * GJOBS + n
                if t > 0:
                    for other in range(2):
                        dve.wait_ge(z_lo_ready[other], t)
                dve.wait_ge(products_hi, job + 1)
                dve.tensor_tensor(gram_lo[:, n * BANK_QUADS:(n + 1) * BANK_QUADS, :], bank_products(job),
                                  gram_hi[:, n * BANK_QUADS:(n + 1) * BANK_QUADS, :].bitcast(F32),
                                  ALU.subtract).then_inc(products_taken, 1)
                if t == 0 and n == 1:
                    dve.memset(z_hi[:].bitcast(F32), 1.0).then_inc(z_filled, 1)
                if t == 0 and n == 3:
                    dve.memset(z_lo[:].bitcast(F32), 0.0).then_inc(z_filled, 1)
                if n == GJOBS - 1:
                    if t == 0:
                        dve.wait_ge(z_filled, 2)
                    pairs_out(dve, dve.tensor_copy, t, 0)

            def l2(t):
                if t == 0:
                    dve.wait_ge(w2_in, 48)
                else:
                    dve.wait_ge(y_ready, t)
                dve.wait_ge(l2_done, t + 1)
                dve.tensor_tensor(h2[:], ps_h2[:, 0:H2], b2_sb[:], ALU.add).then_inc(h2_sum, 1)
                dve.wait_ge(h2_sum, t + 1)
                dve.scalar_tensor_tensor(out=h2w[:], in0=h2[:], scalar=0.0, in1=w3_sb[:], op0=ALU.max, op1=ALU.mult,
                                         accum_out=y[:, t:t + 1]).then_inc(y_ready, 1)

            steps(pick, turn, product, nothing, nothing, l2)

        @block.scalar
        def _(act):
            act.dma_start(ids_sb[:], ids.rearrange("(t p) n -> p t n", p=P)).then_inc(ids_in, 16)

            def take_pick(k):
                wait_picked(act, k)
                act.copy(feat[:, :, :, 1 + NG + k],
                         ps_g[:, bank(k), :].rearrange("p (t b) -> p t b", t=T)).then_inc(picked_taken, 1)

            def split_table(k):
                n, c = splits[k]
                act.wait_ge(table_in[k % 2], 32 * (k // 2 + 1) if n % 16 else 16 * (k // 2 + 1))
                if k >= TABLES:
                    wait_picked(act, k - TABLES)
                act.copy(table_hi[0:n, k % TABLES, 0:c * D], table[0:n, k % 2, 0:c * D]).then_inc(hi_ready, 1)

            def build_onehot(k):
                n, c = splits[k]
                act.wait_ge(ids_bc_in[k % 2], 16 * (k // 2 + 1))
                for i in range(c - ACT_CHUNKS, c):
                    wait_chunk_free(act, k, i)
                    m = chunks_until(k, i, 1)
                    if m > 1:
                        act.wait_ge(onehot_ready[1], m - 1)
                    act.activation(distance[0:n, :], ids_bc[0:n, k % 2, :], ACT.Abs, bias=row_ids[c][0:n, i:i + 1],
                                   scale=-1.0).then_inc(distance_ready, 1)
                    act.wait_ge(distance_ready, m)
                    act.activation(onehot[0:n, chunk(k, i) % RING, :], distance[0:n, :], ACT.Relu, bias=1.0,
                                   scale=-1.0).then_inc(onehot_ready[1], 1)

            def pick(k):
                if k == 0:
                    split_table(0)
                    act.wait_ge(row_ids_ready, len(row_ids))
                    build_onehot(0)
                if k + 1 < NK:
                    split_table(k + 1)
                    build_onehot(k + 1)
                if k > 0:
                    take_pick(k - 1)
                if k == NK - 1:
                    for n, half in enumerate(halves):
                        act.wait_ge(w1z_in[n], 16)
                        act.copy(w1z_hi[:, half, :], w1z_sb[:, half, :]).then_inc(w1_hi_ready, 1)

            def turn(t, g):
                turned_out(act, act.copy, t, g, 1)

            def product(t, n):
                if t == 0 and n == 0:
                    take_pick(NK - 1)
                job = t * GJOBS + n
                if t > 0:
                    for other in range(2):
                        act.wait_ge(z_hi_ready[other], t)
                act.wait_ge(products, job + 1)
                act.copy(gram_hi[:, n * BANK_QUADS:(n + 1) * BANK_QUADS, :], bank_products(job)).then_inc(products_hi, 1)
                if n == GJOBS - 1:
                    if t == 0:
                        act.wait_ge(z_filled, 2)
                    pairs_out(act, act.copy, t, 1)

            def l1(t):
                act.wait_ge(l1_done, t + 1)
                if t > 0:
                    act.wait_ge(h1_transposed, t)
                act.activation(h1[:], ps_h1[:], ACT.Relu).then_inc(h1_ready, 1)

            def turn_h1(t):
                act.wait_ge(h1_transposed, t + 1)
                if t > 0:
                    act.wait_ge(l2_done, t)
                act.copy(h1t[:], ps_h1t[:]).then_inc(h1t_ready, 1)

            steps(pick, turn, product, l1, turn_h1, nothing)


PICKED = 7


def kernel(**inputs):
    import numpy as np
    import concourse.bacc as bacc
    from concourse import mybir as mb
    from concourse.bass_utils import run_bass_kernel_spmd

    names = [f"tbl_{i}" for i in range(sum(n.startswith("tbl_") for n in inputs))]
    by_size = sorted(range(len(names)), key=lambda i: inputs[names[i]].shape[0])
    picked = sorted(by_size[:PICKED])
    by_gather = sorted(by_size[PICKED:])
    table_of_slot = [None] + by_gather + picked
    nf = len(table_of_slot)

    w1 = np.asarray(inputs["W_top1"])
    first, second = np.triu_indices(nf, k=1)
    pair_at = np.zeros((nf, nf), int)
    pair_at[first, second] = np.arange(len(first))
    feature = np.array([0] + [1 + i for i in table_of_slot[1:]])
    a, b = feature[first], feature[second]
    w1z = np.zeros((128, (nf + 2) // 4, w1.shape[1]), w1.dtype)
    w1z[32 * ((second - 1) % 4) + first, (second - 1) // 4] = w1[pair_at[np.minimum(a, b), np.maximum(a, b)]]
    w1z[nf, 0] = inputs["b_top1"]
    ids = np.asarray(inputs["ids"])
    arrays = {
        "dense": inputs["r_dense"], "ids": ids, "ids_by_table": ids.T[picked],
        **{n: inputs[n] for n in names},
        "w1z": w1z, "w1d": w1[len(first):], "w2": inputs["W_top2"],
        "b2": np.asarray(inputs["b_top2"])[None, :], "w3": np.asarray(inputs["W_top3"]).T,
    }
    arrays = {n: np.ascontiguousarray(x) for n, x in arrays.items()}
    nc = bacc.Bacc("TRN2", target_bir_lowering=False, num_devices=1)
    ap = {n: nc.dram_tensor(n, x.shape, mb.dt.from_np(x.dtype), kind="ExternalInput").ap() for n, x in arrays.items()}
    out = nc.dram_tensor("out", (arrays["dense"].shape[0], 1), mb.dt.float32, kind="ExternalOutput").ap()
    dlrm_tower(nc, ap["dense"], ap["ids"], ap["ids_by_table"], [ap[names[i]] for i in by_gather],
               [ap[names[i]] for i in picked], table_of_slot, ap["w1z"], ap["w1d"], ap["w2"], ap["b2"], ap["w3"], out)
    r = run_bass_kernel_spmd(nc, [arrays], core_ids=[0])
    return r.results[0]["out"]
```

```python
from contextlib import ExitStack

import concourse.bass as bass
from concourse import mybir

F32 = mybir.dt.float32
F32R = mybir.dt.float32r
I32 = mybir.dt.int32
U32 = mybir.dt.uint32
ALU = mybir.AluOpType
ACT = mybir.ActivationFunctionType

P = 128
QUAD = 4
GROUP = 4
EARLY = (3, 5, 6)
WARMING = 10
RAW = 3
TABLES = 3
RING = 12
ACT_CHUNKS = 1
W1_BEFORE = (3, 5)


def table_split(rows):
    n = next(n for n in range(P, 0, -1) if rows % n == 0)
    return n, rows // n


def dlrm_tower(nc, dense, ids, ids_by_table, gathered_tables, picked_tables, table_of_slot,
               w1z, w1d, w2, b2, w3, out):
    B, D = dense.shape
    NG, NK = len(gathered_tables), len(picked_tables)
    NF = 1 + NG + NK
    NM = NF - 1
    T = B // P
    TQ = P // QUAD
    QROW = QUAD * NM
    BANK_QUADS = 512 // QROW
    GJOBS = TQ // BANK_QUADS
    MM = (NM + 3) // 4
    H1, H2 = w2.shape
    C1 = H1 // P
    slots = [list(range(g, min(g + GROUP, 1 + NG))) for g in range(0, 1 + NG, GROUP)]
    TG = len(slots)

    def slots_of(t):
        return slots if t < T - 1 else slots[:-1] + [slots[-1][:-1], slots[-1][-1:]]

    splits = [table_split(tb.shape[0]) for tb in picked_tables]
    KP, CMAX = max(n for n, _ in splits), max(c for _, c in splits)
    W = 32

    with ExitStack() as ctx:
        def sb(name, shape, dt=F32):
            return ctx.enter_context(nc.sbuf_tensor(name, shape, dt))

        def psum(name, shape):
            return ctx.enter_context(nc.psum_tensor(name, shape, F32))

        def sem(name):
            return ctx.enter_context(nc.semaphore(name))

        ids_sb = sb("ids_sb", [P, T, ids.shape[1]], I32)
        rows = sb("rows", [P, 2, 1 + NG, D])
        feat = sb("feat", [P, T, P, W])
        ident = sb("ident", [P, P])
        ones = sb("ones", [P, P])
        w1z_sb = sb("w1z_sb", [P, MM, H1])
        w1z_hi = sb("w1z_hi", [P, MM, H1], F32R)
        w1d_sb = sb("w1d_sb", [P, H1])
        w2_sb = sb("w2_sb", [P, C1, H2])
        b2_sb = sb("b2_sb", [P, H2])
        w3_sb = sb("w3_sb", [P, H2])
        h1 = sb("h1", [P, H1])
        h2 = sb("h2", [P, H2])
        h2w = sb("h2w", [P, H2])
        y = sb("y", [P, T])
        row_ids_int = sb("row_ids_int", [P, CMAX], I32)
        row_ids = {c: sb(f"row_ids_{c}", [P, c]) for c in sorted({c for _, c in splits})}

        with ExitStack() as of_picks:
            def pick_sb(name, shape, dt=F32):
                return of_picks.enter_context(nc.sbuf_tensor(name, shape, dt))

            ids_bc = pick_sb("ids_bc", [P, RAW, B], I32)
            distance = pick_sb("distance", [P, B])
            table = pick_sb("table", [P, RAW, CMAX * D])
            table_hi = pick_sb("table_hi", [P, TABLES, CMAX * D], F32R)
            table_lo = pick_sb("table_lo", [P, TABLES, CMAX * D], F32R)
            onehot = pick_sb("onehot", [P, RING, B], F32R)
        w1z_lo = sb("w1z_lo", [P, MM, H1], F32R)
        gram_hi = sb("gram_hi", [P, TQ, QROW], F32R)
        gram_lo = sb("gram_lo", [P, TQ, QROW], F32R)
        z_hi = sb("z_hi", [P, MM, P], F32R)
        z_lo = sb("z_lo", [P, MM, P], F32R)
        w1d_hi = sb("w1d_hi", [P, H1], F32R)
        w1d_lo = sb("w1d_lo", [P, H1], F32R)
        dense_hi = sb("dense_hi", [P, P], F32R)
        dense_lo = sb("dense_lo", [P, P], F32R)
        w2_hi = sb("w2_hi", [P, C1, H2], F32R)
        w2_lo = sb("w2_lo", [P, C1, H2], F32R)
        h1t_hi = sb("h1t_hi", [P, C1, P], F32R)
        h1t_lo = sb("h1t_lo", [P, C1, P], F32R)

        ps_t = psum("ps_t", [P, 2, GROUP * P])
        ps_g = psum("ps_g", [P, 3, 512])
        ps_h1 = psum("ps_h1", [P, H1])
        ps_h1t = psum("ps_h1t", [P, C1, P])
        ps_h2 = psum("ps_h2", [P, 512])

        ids_in = [sem(f"ids_in_{n}") for n in range(2)]
        ids_bc_in = [sem(f"ids_bc_in_{n}") for n in range(RAW)]
        dense_in = [sem(f"dense_in_{n}") for n in range(2)]
        table_in = [sem(f"table_in_{n}") for n in range(RAW)]
        w1z_in = [sem(f"w1z_in_{n}") for n in range(2)]
        first_half_in = sem("first_half_in")
        w1d_in = sem("w1d_in")
        w2_in = sem("w2_in")
        b2_w3_in = sem("b2_w3_in")
        gathered = [[sem(f"gathered_{t}_{g}") for g in range(len(slots_of(t)))] for t in range(T)]
        ident_zeroed = sem("ident_zeroed")
        ident_ready = sem("ident_ready")
        pads_zeroed = sem("pads_zeroed")
        z_filled = sem("z_filled")
        w1_hi_ready = sem("w1_hi_ready")
        w1_lo_ready = sem("w1_lo_ready")
        ids_made = sem("ids_made")
        row_ids_ready = sem("row_ids_ready")
        ones_ready = sem("ones_ready")
        hi_ready = sem("hi_ready")
        lo_ready = sem("lo_ready")
        first_hi_ready = sem("first_hi_ready")
        first_lo_ready = sem("first_lo_ready")
        onehot_ready = [sem(f"onehot_ready_{n}") for n in range(2)]
        distance_ready = sem("distance_ready")
        onehot_used = sem("onehot_used")
        picked_taken = sem("picked_taken")
        transposed = sem("transposed")
        turned = [sem(f"turned_{n}") for n in range(2)]
        products = sem("products")
        products_hi = sem("products_hi")
        products_taken = sem("products_taken")
        z_hi_ready = [sem(f"z_hi_ready_{n}") for n in range(2)]
        z_lo_ready = [sem(f"z_lo_ready_{n}") for n in range(2)]
        dense_hi_ready = sem("dense_hi_ready")
        dense_lo_ready = sem("dense_lo_ready")
        l1_done = sem("l1_done")
        h1_ready = sem("h1_ready")
        h1_transposed = sem("h1_transposed")
        w1d_hi_ready = sem("w1d_hi_ready")
        w1d_lo_ready = sem("w1d_lo_ready")
        w2_hi_ready = sem("w2_hi_ready")
        w2_lo_ready = sem("w2_lo_ready")
        h1t_hi_ready = sem("h1t_hi_ready")
        h1t_lo_ready = sem("h1t_lo_ready")
        l2_done = sem("l2_done")
        h2_sum = sem("h2_sum")
        y_ready = sem("y_ready")
        out_done = sem("out_done")

        def chunk(k, i):
            return sum(c for _, c in splits[:k]) + i

        def wait_picked(eng, k):
            eng.wait_ge(onehot_used, chunk(k, splits[k][1]))

        def wait_chunk_free(eng, k, i):
            if chunk(k, i) >= RING:
                eng.wait_ge(onehot_used, chunk(k, i) - RING + 1)

        def chunks_until(k, i, who):
            act_from = splits[k][1] - ACT_CHUNKS
            before = sum(splits[j][1] - ACT_CHUNKS if who == 0 else ACT_CHUNKS for j in range(k))
            return before + (min(i + 1, act_from) if who == 0 else max(0, i + 1 - act_from))

        def table_cols(k):
            c = splits[k][1]
            return (slice(0, c // 2 * D), slice(c // 2 * D, c * D)) if k == 0 else (slice(0, c * D),)

        def table_loads(k):
            return sum(32 if splits[j][0] % 16 else 16 for j in range(k % RAW, k + 1, RAW))

        def h1_parts(t):
            return [slice(0, C1)] if t < T - 1 else [slice(0, C1 // 2), slice(C1 // 2, C1)]

        def h1_cols(part):
            return slice(part.start * P, part.stop * P)

        def ps_h1_of(t, n):
            cols = h1_cols(h1_parts(t)[n])
            return ps_h1[:, cols] if n == 0 else ps_t[:, 0, 0:cols.stop - cols.start]

        def ps_h1t_of(t, n):
            part = h1_parts(t)[n]
            if n == 0:
                return ps_h1t[:, part, :]
            return ps_t[:, 1, 0:(part.stop - part.start) * P].rearrange("p (c b) -> p c b", b=P)

        half = GJOBS // 2
        pairs_after = {half: [(0, 0, half, (0, 1))], half + 1: [(0, 0, half, (2, 3))],
                       GJOBS - 1: [(0, half, half, (0, 1, 2, 3)), (1, 0, GJOBS, (0, 1, 2, 3))]}

        halves = (slice(0, MM // 2), slice(MM // 2, MM))

        block = ctx.enter_context(nc.Block())

        def steps(pick, turn, product, l1, turn_h1, l2, is_pe=False):
            for k in range(NK):
                pick(k)
                if 0 < k <= TG:
                    turn(0, k - 1)
            for g in range(NK - 1, TG):
                turn(0, g)
            for t in range(T):
                early = EARLY if 0 < t < T - 2 else EARLY[:-1]
                for n in range(GJOBS):
                    product(t, n)
                    if n == 0 and 0 < t < T - 1:
                        turn_h1(t - 1)
                    if n in early and t + 1 < T:
                        turn(t + 1, early.index(n))
                if t > 0:
                    l2(t - 1)
                if t + 1 < T:
                    for g in range(len(early), TG - 1):
                        turn(t + 1, g)
                l1(t)
                if t + 1 == T - 1 or t + 1 < T and not is_pe:
                    turn(t + 1, TG - 1)
                if t + 1 == T - 1 and is_pe:
                    turn_h1(t)
                if t + 1 == T - 1:
                    turn(t + 1, TG)
                if t + 1 == T - 1 and not is_pe:
                    turn_h1(t)
            turn_h1(T - 1)
            l2(T - 1)

        def nothing(*_):
            pass

        @block.sync
        def _(sp):
            def load_ids(k):
                sp.dma_start(ids_bc[:, k % RAW, :], ids_by_table[k:k + 1, :].to_broadcast([P, B])).then_inc(ids_bc_in[k % RAW], 16)

            def load_table(k):
                n, c = splits[k]
                if k >= RAW:
                    for who in range(2):
                        sp.wait_ge(onehot_ready[who], chunks_until(k - RAW, splits[k - RAW][1] - 1, who))
                    sp.wait_ge(hi_ready, k - RAW + 1)
                    sp.wait_ge(lo_ready, k - RAW + 1)
                if k == 0:
                    load_ids(0)
                src = picked_tables[k].rearrange("(p c) d -> p (c d)", c=c)
                cut = n // 16 * 16
                for part, cols in enumerate(table_cols(k)):
                    loaded = first_half_in if k == 0 and part == 0 else table_in[k % RAW]
                    sp.dma_start(table[0:cut, k % RAW, cols], src[0:cut, cols]).then_inc(loaded, 16)
                    if cut < n:
                        sp.dma_start(table[cut:n, k % RAW, cols], src[cut:n, cols]).then_inc(loaded, 16)
                if k > 0:
                    load_ids(k)

            load_table(0)
            load_table(1)
            for t in range(2):
                sp.dma_start(rows[:, t, 0, :], dense[t * P:(t + 1) * P, :]).then_inc(dense_in[t], 16)
            for k in range(2, NK):
                if k in W1_BEFORE:
                    n = W1_BEFORE.index(k)
                    sp.dma_start(w1z_sb[:, halves[n], :], w1z[:, halves[n], :]).then_inc(w1z_in[n], 16)
                load_table(k)
            sp.dma_start(w1d_sb[:], w1d).then_inc(w1d_in, 16)
            sp.dma_start(w2_sb[:], w2.rearrange("(c p) h -> p c h", p=P)).then_inc(w2_in, 16)
            sp.dma_start(b2_sb[:], b2.to_broadcast([P, H2])).then_inc(b2_w3_in, 16)
            sp.dma_start(w3_sb[:], w3.to_broadcast([P, H2])).then_inc(b2_w3_in, 16)
            for t in range(2, T):
                sp.wait_ge(transposed, TG * (t - 2) + 1)
                sp.dma_start(rows[:, t % 2, 0, :], dense[t * P:(t + 1) * P, :]).then_inc(dense_in[t % 2], 16)
            for t in range(T):
                sp.wait_ge(y_ready, t + 1)
                sp.dma_start(out[t * P:(t + 1) * P, :], y[:, t:t + 1]).then_inc(out_done, 16)
            sp.wait_ge(out_done, 16 * T)

        @block.gpsimd
        def _(pool):
            for n, (c, tile) in enumerate(row_ids.items()):
                if n > 0:
                    pool.wait_ge(row_ids_ready, n)
                pool.iota(row_ids_int[:, 0:c], pattern=[[1, c]], base=0, channel_multiplier=c).then_inc(ids_made, 1)
                pool.wait_ge(ids_made, n + 1)
                pool.tensor_copy(tile[:], row_ids_int[:, 0:c]).then_inc(row_ids_ready, 1)
            pool.memset(ident[:], 0.0).then_inc(ident_zeroed, 1)
            pool.wait_ge(ident_zeroed, 1)
            pool.affine_select(out=ident[:], in_=ident[:], compare_op=ALU.not_equal, fill=1.0, base=0,
                               pattern=[[-1, P]], channel_multiplier=1).then_inc(ident_ready, 1)
            pool.memset(feat[:, T - 1:T, :, NF:W], 0.0).then_inc(pads_zeroed, 1)
            for t in range(T):
                if t < 2:
                    pool.wait_ge(ids_in[t], 16)
                for g, ss in enumerate(slots_of(t)):
                    if t >= 2:
                        pool.wait_ge(transposed, TG * (t - 2) + min(g, TG - 1) + 1)
                    for s in ss:
                        if s > 0:
                            i = table_of_slot[s]
                            pool.indirect_dma_start(
                                out=rows[:, t % 2, s, :], out_offset=None, in_=gathered_tables[s - 1],
                                in_offset=bass.IndirectOffsetOnAxis(ap=ids_sb[:, t, i:i + 1].bitcast(U32), axis=0),
                            ).then_inc(gathered[t][g], 16)

        def bank(job):
            return job % 3

        def wait_bank(eng, job):
            last = job - 3
            if last < 0:
                return
            if last < NK:
                eng.wait_ge(picked_taken, last + 1)
            else:
                eng.wait_ge(products_taken, last - NK + 1)

        def turner(n):
            return 1 if n < TG else (TG - 1 - n % TG) % 2

        def groups_turned(n, who):
            return len([i for i in range(n + 1) if turner(i) == who])

        def wait_turned(eng, n):
            eng.wait_ge(turned[turner(n)], groups_turned(n, turner(n)))

        def turned_out(eng, copy, t, g, who):
            n, ss = t * TG + g, slots_of(t)[g]
            if turner(n) == who:
                eng.wait_ge(transposed, n + 1)
                copy(feat[:, t, :, ss[0]:ss[-1] + 1].rearrange("p b f -> p f b"),
                     ps_t[:, n % 2, 0:len(ss) * P].rearrange("p (f b) -> p f b", b=P)).then_inc(turned[who], 1)

        @block.tensor
        def _(pe):
            pe.wait_ge(ones_ready, 1)
            for _ in range(WARMING):
                pe.matmul(ps_h1[:, 0:P], ones[:], ones[:], start=True, stop=True)

            def pick(k):
                n, c = splits[k]
                if k > 0:
                    pe.wait_ge(hi_ready, k + 1)
                wait_bank(pe, k)
                order = ([(i, 0) for i in range(c)] + [(i, 1) for i in range(c)] if k == 0 else
                         [(i, part) for i in range(c) for part in range(2)])
                for m, (i, part) in enumerate(order):
                    if k == 0 and i in (0, c // 2):
                        pe.wait_ge(((first_hi_ready, hi_ready), (first_lo_ready, lo_ready))[part][int(i > 0)], 1)
                    if part == 0:
                        who = int(i >= c - ACT_CHUNKS)
                        pe.wait_ge(onehot_ready[who], chunks_until(k, i, who))
                    elif k > 0 and i == 0:
                        pe.wait_ge(lo_ready, k + 1)
                    mm = pe.matmul(ps_g[:, bank(k), :], (table_hi, table_lo)[part][0:n, k % TABLES, i * D:(i + 1) * D],
                                   onehot[0:n, chunk(k, i) % RING, :], start=(m == 0), stop=(m == 2 * c - 1))
                    if part == 1:
                        mm.then_inc(onehot_used, 1)

            def turn(t, g):
                n, ss = t * TG + g, slots_of(t)[g]
                if n == 0:
                    pe.wait_ge(ident_ready, 1)
                if g == 0:
                    pe.wait_ge(dense_in[t % 2], 16 * (t // 2 + 1))
                pe.wait_ge(gathered[t][g], 16 * len([s for s in ss if s > 0]))
                if n >= 2:
                    wait_turned(pe, n - 2)
                for i, s in enumerate(ss):
                    last = pe.transpose(ps_t[:, n % 2, i * P:(i + 1) * P], rows[:, t % 2, s, :], ident[:])
                last.then_inc(transposed, 1)

            def product(t, n):
                if n == 0:
                    if t == 0:
                        pe.wait_ge(picked_taken, NK)
                        pe.wait_ge(pads_zeroed, 2)
                    last_group = t * TG + len(slots_of(t)) - 1
                    for who in range(2):
                        pe.wait_ge(turned[who], groups_turned(last_group, who))
                job = NK + t * GJOBS + n
                wait_bank(pe, job)
                for q in range(BANK_QUADS):
                    b = QUAD * (n * BANK_QUADS + q)
                    quad_all = feat[:, t, b:b + QUAD, :].rearrange("p b f -> p (b f)")
                    quad_used = feat[:, t, b:b + QUAD, 1:NF]
                    last = pe.matmul(ps_g[:, bank(job), q * QROW:(q + 1) * QROW], quad_all, quad_used,
                                     start=True, stop=True)
                last.then_inc(products, 1)

            def l1(t):
                if t > 0:
                    pe.wait_ge(h1_ready, t)
                else:
                    pe.wait_ge(w1d_lo_ready, 1)
                pe.wait_ge(dense_lo_ready, t + 1)
                parts = [(ps_h1_of(t, n), h1_cols(part)) for n, part in enumerate(h1_parts(t))]
                for into, cols in parts:
                    for x, w in ((dense_hi, w1d_hi), (dense_hi, w1d_lo), (dense_lo, w1d_hi)):
                        pe.matmul(into, x[:], w[:, cols], start=(x is dense_hi and w is w1d_hi), stop=False)
                if t == 0:
                    pe.wait_ge(w1_lo_ready, 2)
                for ready, z, weights in ((z_hi_ready, z_hi, (w1z_hi, w1z_lo)), (z_lo_ready, z_lo, (w1z_hi,))):
                    for who in range(2):
                        pe.wait_ge(ready[who], t + 1)
                    if z is z_lo and t + 1 == T - 1:
                        turn(t + 1, TG - 2)
                    for into, cols in parts:
                        for mm in range(MM):
                            if z is z_lo and mm == MM // 2 and t + 1 < T - 1:
                                turn(t + 1, TG - 1)
                            for w in weights:
                                last = pe.matmul(into, z[:, mm, :], w[:, mm, cols], start=False,
                                                 stop=(z is z_lo and mm == MM - 1))
                        if z is z_lo:
                            last.then_inc(l1_done, 1)

            def turn_outside_l1(t, g):
                if t < T - 1 or g != TG - 2:
                    turn(t, g)

            def turn_h1(t):
                if t > 0:
                    pe.wait_ge(h1t_lo_ready, t)
                for n, part in enumerate(h1_parts(t)):
                    if n == 1:
                        pe.wait_ge(b2_w3_in, 32)
                        pe.wait_ge(h2_sum, t)
                        pe.matmul(ps_h2[:, 0:H2], ones[0:1, :], b2_sb[0:1, :], start=True, stop=False)
                    pe.wait_ge(h1_ready, t + n + 1)
                    for c in range(part.start, part.stop):
                        last = pe.transpose(ps_h1t_of(t, n)[:, c - part.start, :], h1[:, c * P:(c + 1) * P], ident[:])
                    last.then_inc(h1_transposed, 1)

            def l2(t):
                if t == 0:
                    pe.wait_ge(w2_lo_ready, 1)
                elif t < T - 1:
                    pe.wait_ge(h2_sum, t)
                for ready, part_of_h1t, weights in ((h1t_hi_ready, h1t_hi, (w2_hi, w2_lo)), (h1t_lo_ready, h1t_lo, (w2_hi,))):
                    for n, part in enumerate(h1_parts(t)):
                        pe.wait_ge(ready, t + n + 1)
                        for c in range(part.start, part.stop):
                            for w in weights:
                                last = pe.matmul(ps_h2[:, 0:H2], part_of_h1t[:, c, :], w[:, c, :],
                                                 start=(t < T - 1 and c == 0 and w is w2_hi and part_of_h1t is h1t_hi),
                                                 stop=(c == C1 - 1 and part_of_h1t is h1t_lo))
                last.then_inc(l2_done, 1)

            steps(pick, turn_outside_l1, product, l1, turn_h1, l2, is_pe=True)

        def bank_products(job):
            return ps_g[:, bank(NK + job), 0:BANK_QUADS * QROW].rearrange("p (q c) -> p q c", c=QROW)

        def pairs_by(t, part, s, i):
            return (i + s) % 2 if part == 1 or 0 < t < T - 1 or s < 3 else 0

        def pairs_out(eng, copy, t, n, who, parts_out=(0, 1)):
            for part, first_bank, banks, ss in pairs_after.get(n, ()):
                if part not in parts_out:
                    continue
                gram, z, ready, there = ((gram_hi, z_hi, z_hi_ready, products_hi),
                                         (gram_lo, z_lo, z_lo_ready, products_taken))[part]
                if t > 0:
                    eng.wait_ge(l1_done, t)
                elif part == 0:
                    eng.wait_ge(z_filled, 3)
                eng.wait_ge(there, t * GJOBS + first_bank + banks)
                q0, q1 = first_bank * BANK_QUADS, (first_bank + banks) * BANK_QUADS
                for s in ss:
                    k = len(range(s, NM, 4))
                    for i in range(QUAD):
                        if pairs_by(t, part, s, i) == who:
                            if t > 0:
                                parts = [(NF, 0, k)]
                            elif s == 0 and z is z_hi:
                                parts = [(NF, 0, 1), (W, 1, k)]
                            else:
                                parts = [(W, 0, k)]
                            for rows_out, m, end in parts:
                                src = gram[W * i:W * i + rows_out, q0:q1, i * NM:(i + 1) * NM]
                                src = src[:, :, s + 4 * m:min(NM, s + 4 * end):4]
                                dst = z[W * s:W * s + rows_out, m:end, QUAD * q0:QUAD * q1]
                                dst = dst.rearrange("p m (q i) -> p m q i", i=QUAD)[:, :, :, i]
                                last = copy(dst, src.rearrange("p q m -> p m q"))
                if first_bank + banks == GJOBS:
                    last.then_inc(ready[who], 1)

        @block.vector
        def _(dve):
            def pick(k):
                n, c = splits[k]
                if k == 0:
                    dve.memset(ones[:], 1.0).then_inc(ones_ready, 1)
                    dve.memset(feat[:, 0:T - 1, :, NF:W], 0.0).then_inc(pads_zeroed, 1)
                    dve.wait_ge(row_ids_ready, len(row_ids))
                dve.wait_ge(ids_bc_in[k % RAW], 16 * (k // RAW + 1))
                for i in range(c - ACT_CHUNKS):
                    wait_chunk_free(dve, k, i)
                    dve.tensor_scalar(onehot[0:n, chunk(k, i) % RING, :], ids_bc[0:n, k % RAW, :],
                                      row_ids[c][0:n, i:i + 1], None, ALU.is_equal).then_inc(onehot_ready[0], 1)
                    if i == (c - ACT_CHUNKS - 1 if k == 0 else 1):
                        if k >= TABLES:
                            wait_picked(dve, k - TABLES)
                        for part, cols in enumerate(table_cols(k)):
                            first = k == 0 and part == 0
                            dve.wait_ge(first_hi_ready if first else hi_ready, k + 1)
                            dve.tensor_tensor(table_lo[0:n, k % TABLES, cols], table[0:n, k % RAW, cols],
                                              table_hi[0:n, k % TABLES, cols].bitcast(F32),
                                              ALU.subtract).then_inc(first_lo_ready if first else lo_ready, 1)

            def turn(t, g):
                turned_out(dve, dve.tensor_copy, t, g, 0)

            def split_w1(n):
                dve.wait_ge(w1_hi_ready, n + 1)
                dve.tensor_tensor(w1z_lo[:, halves[n], :], w1z_sb[:, halves[n], :],
                                  w1z_hi[:, halves[n], :].bitcast(F32), ALU.subtract).then_inc(w1_lo_ready, 1)

            def product(t, n):
                if t == 0 and n == 0:
                    for who in range(2):
                        dve.wait_ge(onehot_ready[who], chunks_until(NK - 1, splits[-1][1] - 1, who))
                    dve.wait_ge(lo_ready, NK)
                    split_w1(0)
                    wait_picked(dve, NK - 1)
                    dve.memset(z_hi[0:W, 0, :].bitcast(F32), 1.0).then_inc(z_filled, 1)
                    for z in (z_hi, z_lo):
                        dve.memset(z[W * (NM % 4):P, MM - 1, :].bitcast(F32), 0.0).then_inc(z_filled, 1)
                    split_w1(1)
                job = t * GJOBS + n
                if t > 0:
                    for other in range(2):
                        dve.wait_ge(z_lo_ready[other], t)
                if t == 1 and n == 0:
                    dve.wait_ge(w2_hi_ready, 1)
                    dve.tensor_tensor(w2_lo[:], w2_sb[:], w2_hi[:].bitcast(F32), ALU.subtract).then_inc(w2_lo_ready, 1)
                pairs_out(dve, dve.tensor_copy, t, n, 0, (0,))
                dve.wait_ge(products_hi, job + 1)
                dve.tensor_tensor(gram_lo[:, n * BANK_QUADS:(n + 1) * BANK_QUADS, :], bank_products(job),
                                  gram_hi[:, n * BANK_QUADS:(n + 1) * BANK_QUADS, :].bitcast(F32),
                                  ALU.subtract).then_inc(products_taken, 1)
                if n == 2:
                    if t == 0:
                        dve.wait_ge(w1d_hi_ready, 1)
                        dve.tensor_tensor(w1d_lo[:], w1d_sb[:], w1d_hi[:].bitcast(F32),
                                          ALU.subtract).then_inc(w1d_lo_ready, 1)
                    dve.wait_ge(dense_hi_ready, t + 1)
                    dve.tensor_tensor(dense_lo[:], feat[:, t, :, 0], dense_hi[:].bitcast(F32),
                                      ALU.subtract).then_inc(dense_lo_ready, 1)
                pairs_out(dve, dve.tensor_copy, t, n, 0, (1,))

            def turn_h1(t):
                if t > 0:
                    dve.wait_ge(l2_done, t)
                for n, part in enumerate(h1_parts(t)):
                    dve.wait_ge(h1t_hi_ready, t + n + 1)
                    dve.tensor_tensor(h1t_lo[:, part, :], ps_h1t_of(t, n), h1t_hi[:, part, :].bitcast(F32),
                                      ALU.subtract).then_inc(h1t_lo_ready, 1)

            def l2(t):
                if t == 0:
                    dve.wait_ge(b2_w3_in, 32)
                else:
                    dve.wait_ge(y_ready, t)
                dve.wait_ge(l2_done, t + 1)
                if t < T - 1:
                    dve.tensor_tensor(h2[:], ps_h2[:, 0:H2], b2_sb[:], ALU.add).then_inc(h2_sum, 1)
                    dve.wait_ge(h2_sum, t + 1)
                dve.scalar_tensor_tensor(out=h2w[:], in0=h2[:] if t < T - 1 else ps_h2[:, 0:H2], scalar=0.0,
                                         in1=w3_sb[:], op0=ALU.max, op1=ALU.mult,
                                         accum_out=y[:, t:t + 1]).then_inc(y_ready, 1)

            steps(pick, turn, product, nothing, turn_h1, l2)

        @block.scalar
        def _(act):
            ids_by_tile = ids.rearrange("(t p) n -> p t n", p=P)
            act.dma_start(ids_sb[:, 0:1, :], ids_by_tile[:, 0:1, :]).then_inc(ids_in[0], 16)
            act.dma_start(ids_sb[:, 1:T, :], ids_by_tile[:, 1:T, :]).then_inc(ids_in[1], 16)

            def take_pick(k):
                wait_picked(act, k)
                act.copy(feat[:, :, :, 1 + NG + k],
                         ps_g[:, bank(k), :].rearrange("p (t b) -> p t b", t=T)).then_inc(picked_taken, 1)

            def split_table(k):
                n, c = splits[k]
                if k >= TABLES:
                    wait_picked(act, k - TABLES)
                for part, cols in enumerate(table_cols(k)):
                    first = k == 0 and part == 0
                    act.wait_ge(first_half_in if first else table_in[k % RAW], table_loads(k))
                    act.copy(table_hi[0:n, k % TABLES, cols],
                             table[0:n, k % RAW, cols]).then_inc(first_hi_ready if first else hi_ready, 1)

            def build_onehot(k):
                n, c = splits[k]
                act.wait_ge(ids_bc_in[k % RAW], 16 * (k // RAW + 1))
                for i in range(c - ACT_CHUNKS, c):
                    wait_chunk_free(act, k, i)
                    m = chunks_until(k, i, 1)
                    if m > 1:
                        act.wait_ge(onehot_ready[1], m - 1)
                    act.activation(distance[0:n, :], ids_bc[0:n, k % RAW, :], ACT.Abs, bias=row_ids[c][0:n, i:i + 1],
                                   scale=-1.0).then_inc(distance_ready, 1)
                    act.wait_ge(distance_ready, m)
                    act.activation(onehot[0:n, chunk(k, i) % RING, :], distance[0:n, :], ACT.Relu, bias=1.0,
                                   scale=-1.0).then_inc(onehot_ready[1], 1)

            def split_w1(n):
                act.wait_ge(w1z_in[n], 16)
                act.copy(w1z_hi[:, halves[n], :], w1z_sb[:, halves[n], :]).then_inc(w1_hi_ready, 1)

            def pick(k):
                if k == 0:
                    split_table(0)
                    act.wait_ge(row_ids_ready, len(row_ids))
                    build_onehot(0)
                if k + 1 < NK:
                    split_table(k + 1)
                    build_onehot(k + 1)
                if k > 0:
                    take_pick(k - 1)
                if k >= NK - 2:
                    split_w1(k - (NK - 2))

            def turn(t, g):
                turned_out(act, act.copy, t, g, 1)

            def product(t, n):
                if t == 0 and n == 0:
                    take_pick(NK - 1)
                job = t * GJOBS + n
                if t > 0:
                    for other in range(2):
                        act.wait_ge(z_hi_ready[other], t)
                act.wait_ge(products, job + 1)
                act.copy(gram_hi[:, n * BANK_QUADS:(n + 1) * BANK_QUADS, :], bank_products(job)).then_inc(products_hi, 1)
                if n == 2:
                    if t == 0:
                        act.wait_ge(w1d_in, 16)
                        act.copy(w1d_hi[:], w1d_sb[:]).then_inc(w1d_hi_ready, 1)
                    else:
                        act.wait_ge(l1_done, t)
                    wait_turned(act, t * TG)
                    act.copy(dense_hi[:], feat[:, t, :, 0]).then_inc(dense_hi_ready, 1)
                pairs_out(act, act.copy, t, n, 1)

            def l1(t):
                if t == 0:
                    act.wait_ge(w2_in, 16)
                    act.copy(w2_hi[:], w2_sb[:]).then_inc(w2_hi_ready, 1)
                if t > 0:
                    act.wait_ge(h1_transposed, t)
                for n, part in enumerate(h1_parts(t)):
                    act.wait_ge(l1_done, t + n + 1)
                    act.activation(h1[:, h1_cols(part)], ps_h1_of(t, n), ACT.Relu).then_inc(h1_ready, 1)

            def turn_h1(t):
                if t > 0:
                    act.wait_ge(l2_done, t)
                for n, part in enumerate(h1_parts(t)):
                    act.wait_ge(h1_transposed, t + n + 1)
                    act.copy(h1t_hi[:, part, :], ps_h1t_of(t, n)).then_inc(h1t_hi_ready, 1)

            steps(pick, turn, product, l1, turn_h1, nothing)


PICKED = 7


def kernel(**inputs):
    import numpy as np
    import concourse.bacc as bacc
    from concourse import mybir as mb
    from concourse.bass_utils import run_bass_kernel_spmd

    names = [f"tbl_{i}" for i in range(sum(n.startswith("tbl_") for n in inputs))]
    by_size = sorted(range(len(names)), key=lambda i: inputs[names[i]].shape[0])
    picked = sorted(by_size[:PICKED])
    by_gather = sorted(by_size[PICKED:])
    table_of_slot = [None] + by_gather + picked
    nf = len(table_of_slot)

    w1 = np.asarray(inputs["W_top1"])
    first, second = np.triu_indices(nf, k=1)
    pair_at = np.zeros((nf, nf), int)
    pair_at[first, second] = np.arange(len(first))
    feature = np.array([0] + [1 + i for i in table_of_slot[1:]])
    a, b = feature[first], feature[second]
    w1z = np.zeros((128, (nf + 2) // 4, w1.shape[1]), w1.dtype)
    w1z[32 * ((second - 1) % 4) + first, (second - 1) // 4] = w1[pair_at[np.minimum(a, b), np.maximum(a, b)]]
    w1z[nf, 0] = inputs["b_top1"]
    ids = np.asarray(inputs["ids"])
    arrays = {
        "dense": inputs["r_dense"], "ids": ids, "ids_by_table": ids.T[picked],
        **{n: inputs[n] for n in names},
        "w1z": w1z, "w1d": w1[len(first):], "w2": inputs["W_top2"],
        "b2": np.asarray(inputs["b_top2"])[None, :], "w3": np.asarray(inputs["W_top3"]).T,
    }
    arrays = {n: np.ascontiguousarray(x) for n, x in arrays.items()}
    nc = bacc.Bacc("TRN2", target_bir_lowering=False, num_devices=1)
    ap = {n: nc.dram_tensor(n, x.shape, mb.dt.from_np(x.dtype), kind="ExternalInput").ap() for n, x in arrays.items()}
    out = nc.dram_tensor("out", (arrays["dense"].shape[0], 1), mb.dt.float32, kind="ExternalOutput").ap()
    dlrm_tower(nc, ap["dense"], ap["ids"], ap["ids_by_table"], [ap[names[i]] for i in by_gather],
               [ap[names[i]] for i in picked], table_of_slot, ap["w1z"], ap["w1d"], ap["w2"], ap["b2"], ap["w3"], out)
    r = run_bass_kernel_spmd(nc, [arrays], core_ids=[0])
    return r.results[0]["out"]
```
